# Optimizing a Trainium2 kernel written in Bass

```python
import numpy as np
import jax
import jax.numpy as jnp

def _softmax(x, axis=-1):
    return jax.nn.softmax(x, axis=axis)

def _gelu(x):
    return jax.nn.gelu(x, approximate=True)

def _silu(x):
    return jax.nn.silu(x)

def _sigmoid(x):
    return jax.nn.sigmoid(x)

def _layernorm(x, axis=-1, eps=1e-05):
    m = jnp.mean(x, axis=axis, keepdims=True)
    v = jnp.var(x, axis=axis, keepdims=True)
    return (x - m) / jnp.sqrt(v + eps)

def _scatter_add(tgt, idx, src, axis=0):
    return tgt.at[idx].add(src)

def _segment_sum(src, seg, n):
    return jax.ops.segment_sum(src, seg, n)
kernel_name = 'mk_dlrm_tower_d1_rec_r8_d7e81d'

def setup_inputs(seed: int=0):
    np.random.seed(seed)
    _w = jnp.asarray

    def _rec_inputs():
        import jax
        import jax.numpy as jnp
        _tk = jax.random.key(seed)
        dense_ctx = jax.random.normal(jax.random.fold_in(_tk, 190), (512, 16), jnp.float32)
        ids = jnp.stack([jax.random.randint(jax.random.fold_in(_tk, 200 + f), (512,), 0, v, jnp.int32) for f, v in enumerate([1000, 1000, 1250, 12500, 1000, 1000, 1000, 1000, 1250, 1250, 12500, 1250, 1000, 1000, 12500, 12500, 1000, 12500, 12500, 1000, 1250, 12500, 1250, 12500, 1250, 1000, 1000, 1250, 1250, 1000, 1250, 1250])], axis=1)
        tbl_0 = 0.05 * jax.random.normal(jax.random.fold_in(_tk, 500 + 0), (1000, 256), jnp.float32)
        tbl_1 = 0.05 * jax.random.normal(jax.random.fold_in(_tk, 500 + 1), (1000, 256), jnp.float32)
        tbl_2 = 0.05 * jax.random.normal(jax.random.fold_in(_tk, 500 + 2), (1250, 256), jnp.float32)
        tbl_3 = 0.05 * jax.random.normal(jax.random.fold_in(_tk, 500 + 3), (12500, 256), jnp.float32)
        tbl_4 = 0.05 * jax.random.normal(jax.random.fold_in(_tk, 500 + 4), (1000, 256), jnp.float32)
        tbl_5 = 0.05 * jax.random.normal(jax.random.fold_in(_tk, 500 + 5), (1000, 256), jnp.float32)
        tbl_6 = 0.05 * jax.random.normal(jax.random.fold_in(_tk, 500 + 6), (1000, 256), jnp.float32)
        tbl_7 = 0.05 * jax.random.normal(jax.random.fold_in(_tk, 500 + 7), (1000, 256), jnp.float32)
        tbl_8 = 0.05 * jax.random.normal(jax.random.fold_in(_tk, 500 + 8), (1250, 256), jnp.float32)
        tbl_9 = 0.05 * jax.random.normal(jax.random.fold_in(_tk, 500 + 9), (1250, 256), jnp.float32)
        tbl_10 = 0.05 * jax.random.normal(jax.random.fold_in(_tk, 500 + 10), (12500, 256), jnp.float32)
        tbl_11 = 0.05 * jax.random.normal(jax.random.fold_in(_tk, 500 + 11), (1250, 256), jnp.float32)
        tbl_12 = 0.05 * jax.random.normal(jax.random.fold_in(_tk, 500 + 12), (1000, 256), jnp.float32)
        tbl_13 = 0.05 * jax.random.normal(jax.random.fold_in(_tk, 500 + 13), (1000, 256), jnp.float32)
        tbl_14 = 0.05 * jax.random.normal(jax.random.fold_in(_tk, 500 + 14), (12500, 256), jnp.float32)
        tbl_15 = 0.05 * jax.random.normal(jax.random.fold_in(_tk, 500 + 15), (12500, 256), jnp.float32)
        tbl_16 = 0.05 * jax.random.normal(jax.random.fold_in(_tk, 500 + 16), (1000, 256), jnp.float32)
        tbl_17 = 0.05 * jax.random.normal(jax.random.fold_in(_tk, 500 + 17), (12500, 256), jnp.float32)
        tbl_18 = 0.05 * jax.random.normal(jax.random.fold_in(_tk, 500 + 18), (12500, 256), jnp.float32)
        tbl_19 = 0.05 * jax.random.normal(jax.random.fold_in(_tk, 500 + 19), (1000, 256), jnp.float32)
        tbl_20 = 0.05 * jax.random.normal(jax.random.fold_in(_tk, 500 + 20), (1250, 256), jnp.float32)
        tbl_21 = 0.05 * jax.random.normal(jax.random.fold_in(_tk, 500 + 21), (12500, 256), jnp.float32)
        tbl_22 = 0.05 * jax.random.normal(jax.random.fold_in(_tk, 500 + 22), (1250, 256), jnp.float32)
        tbl_23 = 0.05 * jax.random.normal(jax.random.fold_in(_tk, 500 + 23), (12500, 256), jnp.float32)
        tbl_24 = 0.05 * jax.random.normal(jax.random.fold_in(_tk, 500 + 24), (1250, 256), jnp.float32)
        tbl_25 = 0.05 * jax.random.normal(jax.random.fold_in(_tk, 500 + 25), (1000, 256), jnp.float32)
        tbl_26 = 0.05 * jax.random.normal(jax.random.fold_in(_tk, 500 + 26), (1000, 256), jnp.float32)
        tbl_27 = 0.05 * jax.random.normal(jax.random.fold_in(_tk, 500 + 27), (1250, 256), jnp.float32)
        tbl_28 = 0.05 * jax.random.normal(jax.random.fold_in(_tk, 500 + 28), (1250, 256), jnp.float32)
        tbl_29 = 0.05 * jax.random.normal(jax.random.fold_in(_tk, 500 + 29), (1000, 256), jnp.float32)
        tbl_30 = 0.05 * jax.random.normal(jax.random.fold_in(_tk, 500 + 30), (1250, 256), jnp.float32)
        tbl_31 = 0.05 * jax.random.normal(jax.random.fold_in(_tk, 500 + 31), (1250, 256), jnp.float32)
        _rk = jax.random.fold_in(_tk, 7)
        W_top1 = 0.0441942 * jax.random.normal(jax.random.fold_in(_tk, 801), (512, 512), jnp.float32)
        W_top2 = 0.0441942 * jax.random.normal(jax.random.fold_in(_tk, 802), (512, 256), jnp.float32)
        W_top3 = 0.0625 * jax.random.normal(jax.random.fold_in(_tk, 803), (256, 1), jnp.float32)
        b_top1 = jnp.zeros((512,), jnp.float32)
        b_top2 = jnp.zeros((256,), jnp.float32)
        return (dense_ctx, ids, tbl_0, tbl_1, tbl_2, tbl_3, tbl_4, tbl_5, tbl_6, tbl_7, tbl_8, tbl_9, tbl_10, tbl_11, tbl_12, tbl_13, tbl_14, tbl_15, tbl_16, tbl_17, tbl_18, tbl_19, tbl_20, tbl_21, tbl_22, tbl_23, tbl_24, tbl_25, tbl_26, tbl_27, tbl_28, tbl_29, tbl_30, tbl_31, W_top1, b_top1, W_top2, b_top2, W_top3)
    dense_ctx, ids, tbl_0, tbl_1, tbl_2, tbl_3, tbl_4, tbl_5, tbl_6, tbl_7, tbl_8, tbl_9, tbl_10, tbl_11, tbl_12, tbl_13, tbl_14, tbl_15, tbl_16, tbl_17, tbl_18, tbl_19, tbl_20, tbl_21, tbl_22, tbl_23, tbl_24, tbl_25, tbl_26, tbl_27, tbl_28, tbl_29, tbl_30, tbl_31, W_top1, b_top1, W_top2, b_top2, W_top3 = _rec_inputs()

    def _L0_rec_setup():
        import jax, jax.numpy as jnp
        import numpy as np
        B, N, D = (1024, 32, 256)
        key = jax.random.key(seed)
        x = jax.random.normal(key, (B, N, D), dtype=jnp.float32)
        return {'x': x}
    _L0_rec_all = _L0_rec_setup()
    _L0_rec_in = {k: v for k, v in _L0_rec_all.items() if k in ()}
    del _L0_rec_all
    return {'dense_ctx': dense_ctx, 'ids': ids, 'tbl_0': tbl_0, 'tbl_1': tbl_1, 'tbl_2': tbl_2, 'tbl_3': tbl_3, 'tbl_4': tbl_4, 'tbl_5': tbl_5, 'tbl_6': tbl_6, 'tbl_7': tbl_7, 'tbl_8': tbl_8, 'tbl_9': tbl_9, 'tbl_10': tbl_10, 'tbl_11': tbl_11, 'tbl_12': tbl_12, 'tbl_13': tbl_13, 'tbl_14': tbl_14, 'tbl_15': tbl_15, 'tbl_16': tbl_16, 'tbl_17': tbl_17, 'tbl_18': tbl_18, 'tbl_19': tbl_19, 'tbl_20': tbl_20, 'tbl_21': tbl_21, 'tbl_22': tbl_22, 'tbl_23': tbl_23, 'tbl_24': tbl_24, 'tbl_25': tbl_25, 'tbl_26': tbl_26, 'tbl_27': tbl_27, 'tbl_28': tbl_28, 'tbl_29': tbl_29, 'tbl_30': tbl_30, 'tbl_31': tbl_31, 'W_top1': W_top1, 'b_top1': b_top1, 'W_top2': W_top2, 'b_top2': b_top2, 'W_top3': W_top3}

def reference(dense_ctx, ids, tbl_0, tbl_1, tbl_2, tbl_3, tbl_4, tbl_5, tbl_6, tbl_7, tbl_8, tbl_9, tbl_10, tbl_11, tbl_12, tbl_13, tbl_14, tbl_15, tbl_16, tbl_17, tbl_18, tbl_19, tbl_20, tbl_21, tbl_22, tbl_23, tbl_24, tbl_25, tbl_26, tbl_27, tbl_28, tbl_29, tbl_30, tbl_31, W_top1, b_top1, W_top2, b_top2, W_top3):
    import jax
    import jax.numpy as jnp

    def _L0_rec_ref(x):
        import jax, jax.numpy as jnp
        import numpy as np
        B, N, D = (1024, 32, 256)
        'Second-order feature interaction (DLRM dot interaction).\n\n            Computes dot(x_i, x_j) for all field pairs i < j (self_interaction=False),\n            flattened in row-major upper-triangular order -> [B, N*(N-1)/2].\n            Matches tf.boolean_mask(dot_products, strictly_upper_mask) ordering.\n            '
        b, n, d = x.shape
        iu, ju = jnp.triu_indices(n, k=1)
        dots = jnp.einsum('bnd,bmd->bnm', x, x)
        return dots[:, iu, ju]
    e = jnp.stack([tbl_0[ids[:, 0]], tbl_1[ids[:, 1]], tbl_2[ids[:, 2]], tbl_3[ids[:, 3]], tbl_4[ids[:, 4]], tbl_5[ids[:, 5]], tbl_6[ids[:, 6]], tbl_7[ids[:, 7]], tbl_8[ids[:, 8]], tbl_9[ids[:, 9]], tbl_10[ids[:, 10]], tbl_11[ids[:, 11]], tbl_12[ids[:, 12]], tbl_13[ids[:, 13]], tbl_14[ids[:, 14]], tbl_15[ids[:, 15]], tbl_16[ids[:, 16]], tbl_17[ids[:, 17]], tbl_18[ids[:, 18]], tbl_19[ids[:, 19]], tbl_20[ids[:, 20]], tbl_21[ids[:, 21]], tbl_22[ids[:, 22]], tbl_23[ids[:, 23]], tbl_24[ids[:, 24]], tbl_25[ids[:, 25]], tbl_26[ids[:, 26]], tbl_27[ids[:, 27]], tbl_28[ids[:, 28]], tbl_29[ids[:, 29]], tbl_30[ids[:, 30]], tbl_31[ids[:, 31]]], axis=1)
    z = _L0_rec_ref(e)
    z = z.reshape(z.shape[0], -1)
    h = jnp.concatenate([z, dense_ctx], axis=1)
    h = jnp.maximum(h @ W_top1 + b_top1, 0.0)
    h = jnp.maximum(h @ W_top2 + b_top2, 0.0)
    y = h @ W_top3
    return y

_drawn_inputs = setup_inputs


def setup_inputs(seed=0):
    import zlib

    import numpy as np

    out = dict(_drawn_inputs(seed))
    spreads = {'b_top1': (0.0, 0.1), 'b_top2': (0.0, 0.1)}
    factors = {}
    for name, (base, spread) in spreads.items():
        noise = np.random.default_rng([zlib.crc32(name.encode()), seed]).standard_normal(out[name].shape)
        drawn = base * np.exp(spread * noise) if base else spread * noise
        out[name] = jnp.asarray(drawn.astype(out[name].dtype))
    for name, factor in factors.items():
        out[name] = (out[name] * factor).astype(out[name].dtype)
    return out
```

```python
from contextlib import ExitStack

import concourse.bass as bass
from concourse import mybir

F32 = mybir.dt.float32
F32R = mybir.dt.float32r
I32 = mybir.dt.int32
ALU = mybir.AluOpType
ACT = mybir.ActivationFunctionType

P = 128
QUAD = 32


def table_bases(rows):
    bases, at = [], 0
    for r in rows:
        bases.append(at)
        at += r
    return bases


def dlrm_tower(nc, ids, row_base, tables, dense_t, ident_in, w1_pairs, w1_dense, b1, w2, b2, w3, out):
    BATCH, F = ids.shape
    D = tables.shape[1]
    H1 = w1_pairs.shape[2]
    H2 = w2.shape[1]
    ND = dense_t.shape[0]
    GS = 32
    FPT = P // GS
    TPG = F // FPT
    GROUPS = BATCH // GS
    GPC = P // GS
    CHUNKS = GROUPS // GPC
    KD = D // P
    TPB = 512 // P
    HALVES = TPG // TPB
    UNITS = HALVES * KD
    FPH = F // HALVES
    SPT = P // F
    GT = GS // SPT
    JJ = F // (P // QUAD)
    N1 = H1 // P
    N2 = H2 // P
    SLOTS = GPC * TPG

    with ExitStack() as ctx:
        def sb(name, shape, dt=F32):
            return ctx.enter_context(nc.sbuf_tensor(name, shape, dt))

        def psum(name, shape):
            return ctx.enter_context(nc.psum_tensor(name, shape, F32))

        def sem(name):
            return ctx.enter_context(nc.semaphore(name))

        ids_sb = sb("ids_sb", [P, GROUPS, F], I32)
        base_sb = sb("base_sb", [P, TPG])
        idx = sb("idx", [P, GROUPS * TPG + SLOTS], I32)
        idx_now = sb("idx_now", [P, SLOTS], I32)
        ident = sb("ident", [P, P])
        rows = sb("rows", [P, SLOTS, D])
        hi = sb("hi", [P, 2, KD, GS * F], F32R)
        lo = sb("lo", [P, 2, KD, GS * F], F32R)
        half_hi = sb("half_hi", [P, 2, KD, GS * F], F32R)
        pairs = sb("pairs", [P, JJ, P])
        w1_sb = sb("w1_sb", [P, JJ, H1])
        w1d_sb = sb("w1d_sb", [ND, H1])
        dense_sb = sb("dense_sb", [ND, BATCH])
        b1_sb = sb("b1_sb", [P, N1])
        w2_sb = sb("w2_sb", [P, N1, H2])
        b2_sb = sb("b2_sb", [P, N2])
        w3_sb = sb("w3_sb", [P, N2])
        h1 = sb("h1", [P, N1, P])
        h2 = sb("h2", [P, N2, P])
        y = sb("y", [1, BATCH])

        turned = psum("turned", [P, UNITS, 512])
        gram = psum("gram", [P, GT, P])
        p1 = psum("p1", [P, N1, P])
        p2 = psum("p2", [P, 4, P])

        ids_in = sem("ids_in")
        base_in = sem("base_in")
        ident_loaded = sem("ident_loaded")
        weights_in = sem("weights_in")
        idx_made = sem("idx_made")
        idx_ready = sem("idx_ready")
        row_in = [sem(f"row_in{s}") for s in range(SLOTS)]
        banks_turned = sem("banks_turned")
        hi_ready = sem("hi_ready")
        banks_split = sem("banks_split")
        grams_done = sem("grams_done")
        pairs_act = sem("pairs_act")
        pairs_dve = sem("pairs_dve")
        p1_done = sem("p1_done")
        h1_ready = sem("h1_ready")
        p2_done = sem("p2_done")
        h2_ready = sem("h2_ready")
        p3_done = sem("p3_done")
        y_ready = sem("y_ready")
        out_done = sem("out_done")

        WEIGHT_DMAS = 7
        block = ctx.enter_context(nc.Block())

        def copy_pairs(copy, k, quadrants):
            for g in quadrants:
                for q in range(P // QUAD):
                    src = gram[QUAD * g:QUAD * (g + 1), :, QUAD * g + JJ * q:QUAD * g + JJ * (q + 1)]
                    dst = pairs[QUAD * q:QUAD * (q + 1), :, k * GS + g:(k + 1) * GS:SPT].rearrange("p j s -> p s j")
                    last = copy(dst, src)
            return last

        def split_view(buf, k, u):
            h, kd = u // KD, u % KD
            return buf[:, k % 2, kd, :].rearrange("p (b f) -> p b f", f=F)[:, :, h * FPH:(h + 1) * FPH]

        def bank_view(u):
            return turned[:, u, :].rearrange("p (f b) -> p b f", b=GS)

        @block.sync
        def _(sp):
            ids_grouped = ids.rearrange("(g b) f -> b g f", b=GS)
            for k in range(FPT):
                sp.dma_start(ids_sb[GS * k:GS * (k + 1), :, :], ids_grouped).then_inc(ids_in, 16)
            sp.dma_start(w1_sb[:, :, :], w1_pairs).then_inc(weights_in, 16)
            sp.dma_start(w2_sb[:, :, :], w2.rearrange("(k p) n -> p k n", p=P)).then_inc(weights_in, 16)
            sp.wait_ge(y_ready, 1 + CHUNKS)
            sp.dma_start(out, y[:, :]).then_inc(out_done, 16)
            sp.wait_ge(out_done, 16)

        @block.gpsimd
        def _(pool):
            with pool.Fori(0, CHUNKS) as c:
                for k in range(GPC):
                    pool.wait_ge(idx_ready, c * GPC + k + 1)
                    nc.gpsimd.nop(nofuse=True)
                    for s in range(k * TPG, (k + 1) * TPG):
                        pool.indirect_dma_start(
                            rows[:, s, :], None, tables,
                            bass.IndirectOffsetOnAxis(idx_now[:, s:s + 1], 0)).then_inc(row_in[s], 16)

        @block.tensor
        def _(pe):
            nc.tensor.sem_inc(grams_done, 2)
            nc.tensor.sem_inc(p1_done, 1)
            pe.wait_ge(ident_loaded, 16)
            with pe.Fori(0, CHUNKS) as c:
                for k in range(GPC):
                    for u in range(UNITS):
                        h, kd = u // KD, u % KD
                        pe.wait_ge(banks_split, c * (GPC * UNITS) + k * UNITS + u + 1)
                        for t in range(TPB):
                            s = k * TPG + h * TPB + t
                            if kd == 0:
                                pe.wait_ge(row_in[s], c * 16 + 16)
                            last = nc.tensor.transpose(turned[:, u, t * P:(t + 1) * P],
                                                       rows[:, s, kd * P:(kd + 1) * P], ident[:, :])
                        last.then_inc(banks_turned, 1)
                    pe.wait_ge(banks_split, c * (GPC * UNITS) + (k + 2) * UNITS)
                    pe.wait_ge(pairs_act, c * GPC + k + 1)
                    pe.wait_ge(pairs_dve, c * GPC + k + 1)
                    for s in range(GT):
                        cols = slice(s * P, (s + 1) * P)
                        for kd in range(KD):
                            nc.tensor.matmul(gram[:, s, :], hi[:, k % 2, kd, cols], half_hi[:, k % 2, kd, cols],
                                             start=(kd == 0), stop=False)
                            last = nc.tensor.matmul(gram[:, s, :], hi[:, k % 2, kd, cols], lo[:, k % 2, kd, cols],
                                                    start=False, stop=(kd == KD - 1))
                    last.then_inc(grams_done, 1)
                pe.wait_ge(weights_in, 16 * WEIGHT_DMAS)
                pe.wait_ge(pairs_act, c * GPC + GPC + 1)
                pe.wait_ge(pairs_dve, c * GPC + GPC + 1)
                for n in range(N1):
                    ncols = slice(n * P, (n + 1) * P)
                    nc.tensor.matmul(p1[:, n, :], w1d_sb[:, ncols], dense_sb[:, bass.ds(c * P, P)],
                                     start=True, stop=False)
                    for jj in range(JJ):
                        last = nc.tensor.matmul(p1[:, n, :], w1_sb[:, jj, ncols], pairs[:, jj, :],
                                                start=False, stop=(jj == JJ - 1))
                last.then_inc(p1_done, 1)
                pe.wait_ge(h1_ready, c + 1)
                pe.wait_ge(y_ready, c + 1)
                for n in range(N2):
                    for kk in range(N1):
                        last = nc.tensor.matmul(p2[:, n, :], w2_sb[:, kk, n * P:(n + 1) * P], h1[:, kk, :],
                                                start=(kk == 0), stop=(kk == N1 - 1))
                last.then_inc(p2_done, 1)
                pe.wait_ge(h2_ready, c + 1)
                for kk in range(N2):
                    last = nc.tensor.matmul(p2[0:1, 2, :], w3_sb[:, kk:kk + 1], h2[:, kk, :],
                                            start=(kk == 0), stop=(kk == N2 - 1))
                last.then_inc(p3_done, 1)

        @block.scalar
        def _(act):
            act.dma_start(base_sb[:, :], row_base).then_inc(base_in, 16)
            act.dma_start(ident[:, :], ident_in).then_inc(ident_loaded, 16)
            act.dma_start(dense_sb[:, :], dense_t).then_inc(weights_in, 16)
            act.dma_start(w1d_sb[:, :], w1_dense).then_inc(weights_in, 16)
            act.dma_start(b1_sb[:, :], b1).then_inc(weights_in, 16)
            act.dma_start(b2_sb[:, :], b2).then_inc(weights_in, 16)
            act.dma_start(w3_sb[:, :], w3).then_inc(weights_in, 16)
            nc.scalar.sem_inc(pairs_act, 1)
            with act.Fori(0, CHUNKS) as c:
                for k in range(GPC):
                    act.wait_ge(grams_done, c * GPC + k + 1)
                    for u in range(UNITS):
                        act.wait_ge(banks_turned, c * (GPC * UNITS) + k * UNITS + u + 1)
                        nc.scalar.activation(split_view(hi, k, u), bank_view(u), ACT.Copy).then_inc(hi_ready, 1)
                    act.wait_ge(grams_done, c * GPC + k + 3)
                    if k == 0:
                        act.wait_ge(p1_done, c + 1)
                    copy_pairs(lambda dst, src: nc.scalar.activation(dst, src, ACT.Copy),
                               k, (0, 1)).then_inc(pairs_act, 1)

        @block.vector
        def _(dve):
            nc.vector.sem_inc(banks_split, UNITS)
            nc.vector.sem_inc(pairs_dve, 1)
            nc.vector.sem_inc(y_ready, 1)
            dve.wait_ge(ids_in, 16 * FPT)
            dve.wait_ge(base_in, 16)
            nc.vector.memset(idx[:, GROUPS * TPG:], 0)
            for k in range(FPT):
                part = slice(GS * k, GS * (k + 1))
                last = nc.vector.tensor_tensor(
                    idx[part, :GROUPS * TPG].rearrange("p (g t) -> p g t", t=TPG), ids_sb[part, :, k:F:FPT],
                    base_sb[part, None, :].broadcast_to([GS, GROUPS, TPG]), ALU.add)
            last.then_inc(idx_made, 1)
            dve.wait_ge(idx_made, 1)
            nc.vector.tensor_copy(idx_now[:, :], idx[:, 0:SLOTS]).then_inc(idx_ready, GPC)
            with dve.Fori(0, CHUNKS) as c:
                for k in range(GPC):
                    for u in range(UNITS):
                        dve.wait_ge(hi_ready, c * (GPC * UNITS) + k * UNITS + u + 1)
                        nc.vector.tensor_scalar(split_view(half_hi, k, u), split_view(hi, k, u).bitcast(F32),
                                                0.5, None, ALU.mult)
                        nc.vector.tensor_tensor(split_view(lo, k, u), bank_view(u), split_view(hi, k, u).bitcast(F32),
                                                ALU.subtract).then_inc(banks_split, 1)
                    nc.vector.tensor_copy(idx_now[:, k * TPG:(k + 1) * TPG],
                                          idx[:, bass.ds(c * SLOTS + SLOTS + k * TPG, TPG)]).then_inc(idx_ready, 1)
                    dve.wait_ge(grams_done, c * GPC + k + 3)
                    if k == 0:
                        dve.wait_ge(p1_done, c + 1)
                    copy_pairs(nc.vector.tensor_copy, k, (2, 3)).then_inc(pairs_dve, 1)
                dve.wait_ge(weights_in, 16 * WEIGHT_DMAS)
                dve.wait_ge(p1_done, c + 2)
                for n in range(N1):
                    last = nc.vector.tensor_scalar(h1[:, n, :], p1[:, n, :], b1_sb[:, n:n + 1], 0.0, ALU.add, ALU.max)
                last.then_inc(h1_ready, 1)
                dve.wait_ge(p2_done, c + 1)
                for n in range(N2):
                    last = nc.vector.tensor_scalar(h2[:, n, :], p2[:, n, :], b2_sb[:, n:n + 1], 0.0, ALU.add, ALU.max)
                last.then_inc(h2_ready, 1)
                dve.wait_ge(p3_done, c + 1)
                nc.vector.tensor_copy(y[:, bass.ds(c * P, P)], p2[0:1, 2, :]).then_inc(y_ready, 1)


def kernel(**inputs):
    import numpy as np
    import concourse.bacc as bacc
    from concourse.bass_utils import run_bass_kernel_spmd

    ids = np.asarray(inputs["ids"])
    fields = ids.shape[1]
    tables = [np.asarray(inputs[f"tbl_{f}"]) for f in range(fields)]
    w1, w2, w3 = (np.asarray(inputs[f"W_top{n}"]) for n in (1, 2, 3))
    n_pairs = fields * (fields - 1) // 2
    per_gather = P // QUAD
    row_base = np.repeat(np.array(table_bases([len(t) for t in tables]), np.float32)
                         .reshape(-1, per_gather).T, QUAD, axis=0)
    i, j = np.indices((fields, fields))
    a, b = np.minimum(i, j), np.maximum(i, j)
    row = np.where(i == j, n_pairs, a * fields - a * (a + 1) // 2 + b - a - 1)
    padded = np.concatenate([w1[:n_pairs], np.zeros((1, w1.shape[1]), w1.dtype)])
    order = row.reshape(fields, P // QUAD, -1).transpose(1, 0, 2).reshape(P, -1)

    arrays = {
        "ids": ids,
        "row_base": row_base,
        "tables": np.concatenate(tables),
        "dense_t": np.ascontiguousarray(np.asarray(inputs["dense_ctx"]).T),
        "identity": np.eye(P, dtype=np.float32),
        "w1_pairs": padded[order],
        "w1_dense": w1[n_pairs:],
        "b1": np.ascontiguousarray(np.asarray(inputs["b_top1"]).reshape(-1, P).T),
        "w2": w2,
        "b2": np.ascontiguousarray(np.asarray(inputs["b_top2"]).reshape(-1, P).T),
        "w3": np.ascontiguousarray(w3[:, 0].reshape(-1, P).T),
    }
    nc = bacc.Bacc("TRN2", target_bir_lowering=False, num_devices=1)
    args = [nc.dram_tensor(name, a.shape, mybir.dt.from_np(a.dtype), kind="ExternalInput").ap()
            for name, a in arrays.items()]
    out = nc.dram_tensor("out", (1, ids.shape[0]), F32, kind="ExternalOutput").ap()
    dlrm_tower(nc, *args, out)
    result = run_bass_kernel_spmd(nc, [arrays], core_ids=[0]).results[0]["out"]
    return result.reshape(-1, 1)
```

```python
from contextlib import ExitStack

import concourse.bass as bass
from concourse import mybir

F32 = mybir.dt.float32
F32R = mybir.dt.float32r
I32 = mybir.dt.int32
ALU = mybir.AluOpType
ACT = mybir.ActivationFunctionType

P = 128
QUAD = 32


def table_bases(rows):
    bases, at = [], 0
    for r in rows:
        bases.append(at)
        at += r
    return bases


def dlrm_tower(nc, ids, row_base, tables, dense_t, identity, w1_pairs, w1_dense, b1, w2, b2, w3, out):
    BATCH, F = ids.shape
    D = tables.shape[1]
    H1 = w1_pairs.shape[2]
    H2 = w2.shape[1]
    ND = dense_t.shape[0]
    SPT = P // F
    TILES = BATCH // SPT
    TPU, TPQ, TPC = 2, 4, P // SPT
    UPC, QPC = TPC // TPU, TPC // TPQ
    CHUNKS = TILES // TPC
    KD = D // P
    JJ = F // (P // QUAD)
    N1, N2 = H1 // P, H2 // P
    SPLIT_TILES = 4 * TPQ
    LAG = 2 * TPU
    IDX_GROUP = 4 * TPU
    EARLY_QUADS = 5
    L1_STEP, L1_PER_STEP = 8, 2
    L2_STEP, L3_STEP = 28, 31
    L1_MATMULS = N1 * (JJ + 1)
    assert D == 2 * P and F == QUAD and H1 == 4 * P and TILES == P and L1_STEP + L1_MATMULS // L1_PER_STEP < L2_STEP

    with ExitStack() as ctx:
        def sb(name, shape, dt=F32):
            return ctx.enter_context(nc.sbuf_tensor(name, shape, dt))

        def psum(name, shape):
            return ctx.enter_context(nc.psum_tensor(name, shape, F32))

        def sem(name):
            return ctx.enter_context(nc.semaphore(name))

        ids_sb = sb("ids_sb", [TILES, P], I32)
        ids_f = sb("ids_f", [TILES, P])
        base_sb = sb("base_sb", [P, 1])
        idx = sb("idx", [P, TILES + TPC], I32)
        idx_now = sb("idx_now", [P, TPC], I32)
        ident = sb("ident", [P, P])
        rows = sb("rows", [P, TPC, D])
        hi_lo = sb("hi_lo", [P, SPLIT_TILES * KD, 2, P], F32R)
        hi_hi = sb("hi_hi", [P, 2, TPQ, P])
        sums = sb("sums", [P, TPC, P])
        pairs = sb("pairs", [P, JJ, P])
        w1_sb = sb("w1_sb", [P, JJ, H1])
        w1d_sb = sb("w1d_sb", [ND, H1])
        dense_sb = sb("dense_sb", [ND, BATCH])
        b1_sb = sb("b1_sb", [P, N1])
        w2_sb = sb("w2_sb", [P, N1, H2])
        b2_sb = sb("b2_sb", [P, N2])
        w3_sb = sb("w3_sb", [P, N2])
        h1 = sb("h1", [P, N1, P])
        h2 = sb("h2", [P, N2, P])
        y = sb("y", [1, BATCH])

        turned = psum("turned", [P, 2, TPU * KD, P])
        gram = psum("gram", [P, 2, TPQ, 2, P])
        p1 = psum("p1", [P, N1, P])
        p2 = psum("p2", [P, 4, P])

        ids_in = sem("ids_in")
        base_in = sem("base_in")
        ident_in = sem("ident_in")
        weights_in = sem("weights_in")
        ids_float = sem("ids_float")
        ids_turned = sem("ids_turned")
        idx_made = sem("idx_made")
        idx_ready = sem("idx_ready")
        row_in = [sem(f"row_in{s}") for s in range(TPC)]
        units_turned = sem("units_turned")
        units_rounded = sem("units_rounded")
        units_split = sem("units_split")
        quads_multiplied = sem("quads_multiplied")
        quads_copied = sem("quads_copied")
        quads_summed = sem("quads_summed")
        moved_act = sem("moved_act")
        moved_dve = sem("moved_dve")
        p1_done = sem("p1_done")
        h1_ready = sem("h1_ready")
        p2_done = sem("p2_done")
        h2_ready = sem("h2_ready")
        p3_done = sem("p3_done")
        y_ready = sem("y_ready")
        out_done = sem("out_done")
        SPLIT_START, SUM_START, MUL_START = 2, 2, SPLIT_TILES // TPQ
        WEIGHT_DMAS = 7
        block = ctx.enter_context(nc.Block())

        def move_pairs(copy, part, quadrants):
            t0, t1 = ((0, EARLY_QUADS * TPQ), (EARLY_QUADS * TPQ, TPC))[part]
            for g in quadrants:
                for q in range(P // QUAD):
                    src = sums[QUAD * g:QUAD * (g + 1), t0:t1, QUAD * g + JJ * q:QUAD * g + JJ * (q + 1)]
                    dst = pairs[QUAD * q:QUAD * (q + 1), :, SPT * t0 + g:SPT * t1:SPT].rearrange("p j t -> p t j")
                    last = copy(dst, src)
            return last

        def split_part(u, which):
            at = (u * TPU % SPLIT_TILES) * KD
            return hi_lo[:, at:at + TPU * KD, which, :]

        @block.sync
        def _(sp):
            sp.dma_start(ids_sb[:, :], ids.rearrange("(t b) f -> t (b f)", b=SPT)).then_inc(ids_in, 16)
            sp.dma_start(base_sb[:, :], row_base).then_inc(base_in, 16)
            sp.dma_start(w1_sb[:, :, :], w1_pairs).then_inc(weights_in, 16)
            sp.dma_start(w2_sb[:, :, :], w2.rearrange("(k p) n -> p k n", p=P)).then_inc(weights_in, 16)
            sp.wait_ge(y_ready, 1 + CHUNKS)
            sp.dma_start(out, y[:, :]).then_inc(out_done, 16)
            sp.wait_ge(out_done, 16)

        @block.gpsimd
        def _(pool):
            with pool.Fori(0, CHUNKS) as c:
                for s in range(TPC):
                    if s % IDX_GROUP == 0:
                        pool.wait_ge(idx_ready, c * (TPC // IDX_GROUP) + s // IDX_GROUP + 1)
                        nc.gpsimd.nop(nofuse=True)
                    pool.indirect_dma_start(rows[:, s, :], None, tables,
                                            bass.IndirectOffsetOnAxis(idx_now[:, s:s + 1], 0)).then_inc(row_in[s], 16)

        @block.tensor
        def _(pe):
            def turn(c, t):
                unit = c * UPC + t // TPU
                if t % TPU == 0:
                    pe.wait_ge(units_split, unit + 1)
                pe.wait_ge(row_in[t], c * 16 + 16)
                for kd in range(KD):
                    last = nc.tensor.transpose(turned[:, t // TPU % 2, t % TPU * KD + kd, :],
                                               rows[:, t, kd * P:(kd + 1) * P], ident[:, :])
                if t % TPU == TPU - 1:
                    last.then_inc(units_turned, 1)

            def multiply(c, t):
                if t % TPU == 0:
                    pe.wait_ge(units_split, c * UPC + (SPLIT_START + t // TPU + 1))
                if t % TPQ == 0:
                    pe.wait_ge(quads_summed, c * QPC + t // TPQ + 1)
                for kd in range(KD):
                    at = (t % SPLIT_TILES) * KD + kd
                    last = nc.tensor.matmul(gram[:, t // TPQ % 2, t % TPQ, :, :].rearrange("p a b -> p (a b)"),
                                            hi_lo[:, at, 0, :], hi_lo[:, at, :, :].rearrange("p a b -> p (a b)"),
                                            start=(kd == 0), stop=(kd == KD - 1))
                if t % TPQ == TPQ - 1:
                    last.then_inc(quads_multiplied, 1)

            def first_layer(c, m0, m1):
                for m in range(m0, min(m1, L1_MATMULS)):
                    if m == 0:
                        pe.wait_ge(weights_in, 16 * WEIGHT_DMAS)
                        pe.wait_ge(moved_act, c * 2 + 2)
                        pe.wait_ge(moved_dve, c * 2 + 2)
                    n, k = m // (JJ + 1), m % (JJ + 1)
                    cols = slice(n * P, (n + 1) * P)
                    if k == 0:
                        nc.tensor.matmul(p1[:, n, :], w1d_sb[:, cols], dense_sb[:, bass.ds(c * P, P)],
                                         start=True, stop=False)
                        continue
                    last = nc.tensor.matmul(p1[:, n, :], w1_sb[:, k - 1, cols], pairs[:, k - 1, :],
                                            start=False, stop=(k == JJ))
                    if m == L1_MATMULS - 1:
                        last.then_inc(p1_done, 1)

            def second_layer(c):
                pe.wait_ge(h1_ready, c + 1)
                pe.wait_ge(y_ready, c + 1)
                for n in range(N2):
                    for k in range(N1):
                        last = nc.tensor.matmul(p2[:, n, :], w2_sb[:, k, n * P:(n + 1) * P], h1[:, k, :],
                                                start=(k == 0), stop=(k == N1 - 1))
                last.then_inc(p2_done, 1)

            def third_layer(c):
                pe.wait_ge(h2_ready, c + 1)
                for k in range(N2):
                    last = nc.tensor.matmul(p2[0:1, 2, :], w3_sb[:, k:k + 1], h2[:, k, :],
                                            start=(k == 0), stop=(k == N2 - 1))
                last.then_inc(p3_done, 1)

            def chunk(c, first):
                for t in range(TPC):
                    turn(c, t)
                    if t >= LAG:
                        multiply(c, t - LAG)
                    elif not first:
                        multiply(c - 1, t - LAG + TPC)
                    if not first and t >= L1_STEP:
                        m = (t - L1_STEP) * L1_PER_STEP
                        first_layer(c - 1, m, m + L1_PER_STEP)
                    if not first and t == L2_STEP:
                        second_layer(c - 1)
                    if not first and t == L3_STEP:
                        third_layer(c - 1)

            nc.tensor.sem_inc(quads_multiplied, MUL_START)
            nc.tensor.sem_inc(p1_done, 1)
            pe.wait_ge(ident_in, 16)
            pe.wait_ge(ids_float, 1)
            nc.tensor.transpose(p2[:, 3, :], ids_f[:, :], ident[:, :]).then_inc(ids_turned, 1)
            chunk(0, True)
            with pe.Fori(1, CHUNKS) as c:
                chunk(c, False)
            for t in range(TPC - LAG, TPC):
                multiply(CHUNKS - 1, t)
            first_layer(CHUNKS - 1, 0, L1_MATMULS)
            second_layer(CHUNKS - 1)
            third_layer(CHUNKS - 1)


        @block.scalar
        def _(act):
            def copy(dst, src):
                return nc.scalar.activation(dst, src, ACT.Copy)

            def round_unit(c, u):
                if u % 2 == 0:
                    act.wait_ge(quads_multiplied, c * QPC + u // 2 + 1)
                act.wait_ge(units_turned, c * UPC + u + 1)
                copy(split_part(u, 0), turned[:, u % 2, :, :]).then_inc(units_rounded, 1)

            def copy_quad(c, q):
                act.wait_ge(quads_summed, c * QPC + q + 1)
                act.wait_ge(quads_multiplied, c * QPC + (MUL_START + q + 1))
                copy(hi_hi[:, q % 2, :, :], gram[:, q % 2, :, 0, :]).then_inc(quads_copied, 1)

            def move(c, part):
                if part == 0:
                    act.wait_ge(p1_done, c + 1)
                act.wait_ge(quads_summed, c * QPC + (SUM_START + (EARLY_QUADS, QPC)[part]))
                move_pairs(copy, part, (0, 1)).then_inc(moved_act, 1)

            def chunk(c, first):
                for u in range(UPC):
                    round_unit(c, u)
                    if u % 2 == 1 and u >= 3:
                        copy_quad(c, (u - 3) // 2)
                    if u == 1 and not first:
                        copy_quad(c - 1, QPC - 1)
                    if u == 2 and not first:
                        move(c - 1, 1)
                    if u == 14:
                        move(c, 0)

            act.dma_start(ident[:, :], identity).then_inc(ident_in, 16)
            act.dma_start(dense_sb[:, :], dense_t).then_inc(weights_in, 16)
            act.dma_start(w1d_sb[:, :], w1_dense).then_inc(weights_in, 16)
            act.dma_start(b1_sb[:, :], b1).then_inc(weights_in, 16)
            act.dma_start(b2_sb[:, :], b2).then_inc(weights_in, 16)
            act.dma_start(w3_sb[:, :], w3).then_inc(weights_in, 16)
            chunk(0, True)
            with act.Fori(1, CHUNKS) as c:
                chunk(c, False)
            copy_quad(CHUNKS - 1, QPC - 1)
            move(CHUNKS - 1, 1)

        @block.vector
        def _(dve):
            def split_unit(c, u):
                dve.wait_ge(units_rounded, c * UPC + u + 1)
                nc.vector.tensor_tensor(split_part(u, 1), turned[:, u % 2, :, :], split_part(u, 0).bitcast(F32),
                                        ALU.subtract).then_inc(units_split, 1)

            def renew_idx(c, g):
                nc.vector.tensor_copy(idx_now[:, g * IDX_GROUP:(g + 1) * IDX_GROUP],
                                      idx[:, bass.ds(c * TPC + (TPC + g * IDX_GROUP), IDX_GROUP)]
                                      ).then_inc(idx_ready, 1)

            def sum_quad(c, q, first):
                if not first and q == 0:
                    dve.wait_ge(moved_act, c * 2 - 1)
                if not first and q == EARLY_QUADS:
                    dve.wait_ge(moved_act, c * 2)
                dve.wait_ge(quads_copied, c * QPC + q + 1)
                nc.vector.scalar_tensor_tensor(out=sums[:, q * TPQ:(q + 1) * TPQ, :], in0=hi_hi[:, q % 2, :, :],
                                               scalar=0.5, in1=gram[:, q % 2, :, 1, :], op0=ALU.mult,
                                               op1=ALU.add).then_inc(quads_summed, 1)

            def move(c, part):
                if part == 0:
                    dve.wait_ge(p1_done, c + 1)
                dve.wait_ge(quads_summed, c * QPC + (SUM_START + (EARLY_QUADS, QPC)[part]))
                move_pairs(nc.vector.tensor_copy, part, (2, 3)).then_inc(moved_dve, 1)

            def bias_relu(dst, src, bias, n_cols):
                for n in range(n_cols):
                    last = nc.vector.tensor_scalar(dst[:, n, :], src[:, n, :], bias[:, n:n + 1], 0.0, ALU.add, ALU.max)
                return last

            def finish_h1(c):
                dve.wait_ge(p1_done, c + 2)
                bias_relu(h1, p1, b1_sb, N1).then_inc(h1_ready, 1)

            def finish_h2(c):
                dve.wait_ge(p2_done, c + 1)
                bias_relu(h2, p2, b2_sb, N2).then_inc(h2_ready, 1)

            def finish_y(c):
                dve.wait_ge(p3_done, c + 1)
                nc.vector.tensor_copy(y[:, bass.ds(c * P, P)], p2[0:1, 2, :]).then_inc(y_ready, 1)

            def chunk(c, first):
                for u in range(UPC):
                    split_unit(c, u)
                    if (u + 1) * TPU % IDX_GROUP == 0:
                        renew_idx(c, (u + 1) * TPU // IDX_GROUP - 1)
                    if u % 2 == 1 and u >= 3:
                        sum_quad(c, (u - 3) // 2, first)
                    if u == 1 and not first:
                        sum_quad(c - 1, QPC - 1, False)
                        move(c - 1, 1)
                    if u == L2_STEP // TPU - 2 and not first:
                        dve.wait_ge(weights_in, 16 * WEIGHT_DMAS)
                        finish_h1(c - 1)
                    if u == L2_STEP // TPU and not first:
                        finish_h2(c - 1)
                    if u == 14:
                        move(c, 0)
                    if u == UPC - 1 and not first:
                        finish_y(c - 1)

            nc.vector.sem_inc(units_split, SPLIT_START)
            nc.vector.sem_inc(quads_summed, SUM_START)
            nc.vector.sem_inc(y_ready, 1)
            nc.vector.memset(idx[:, TILES:], 0)
            dve.wait_ge(ids_in, 16)
            nc.vector.tensor_copy(ids_f[:, :], ids_sb[:, :]).then_inc(ids_float, 1)
            dve.wait_ge(ids_turned, 1)
            dve.wait_ge(base_in, 16)
            nc.vector.tensor_scalar(idx[:, 0:TILES], p2[:, 3, :], base_sb[:, 0:1], None, ALU.add).then_inc(idx_made, 1)
            dve.wait_ge(idx_made, 1)
            nc.vector.tensor_copy(idx_now[:, :], idx[:, 0:TPC]).then_inc(idx_ready, TPC // IDX_GROUP)
            chunk(0, True)
            with dve.Fori(1, CHUNKS) as c:
                chunk(c, False)
            sum_quad(CHUNKS - 1, QPC - 1, False)
            move(CHUNKS - 1, 1)
            finish_h1(CHUNKS - 1)
            finish_h2(CHUNKS - 1)
            finish_y(CHUNKS - 1)


def kernel(**inputs):
    import numpy as np
    import concourse.bacc as bacc
    from concourse.bass_utils import run_bass_kernel_spmd

    ids = np.asarray(inputs["ids"])
    fields = ids.shape[1]
    tables = [np.asarray(inputs[f"tbl_{f}"]) for f in range(fields)]
    w1, w2, w3 = (np.asarray(inputs[f"W_top{n}"]) for n in (1, 2, 3))
    n_pairs = fields * (fields - 1) // 2
    row_base = np.tile(np.array(table_bases([len(t) for t in tables]), np.float32), P // fields)[:, None]
    i, j = np.indices((fields, fields))
    a, b = np.minimum(i, j), np.maximum(i, j)
    row = np.where(i == j, n_pairs, a * fields - a * (a + 1) // 2 + b - a - 1)
    padded = np.concatenate([w1[:n_pairs], np.zeros((1, w1.shape[1]), w1.dtype)])
    order = row.reshape(fields, P // QUAD, -1).transpose(1, 0, 2).reshape(P, -1)

    arrays = {
        "ids": ids,
        "row_base": row_base,
        "tables": np.concatenate(tables),
        "dense_t": np.ascontiguousarray(np.asarray(inputs["dense_ctx"]).T),
        "identity": np.eye(P, dtype=np.float32),
        "w1_pairs": padded[order],
        "w1_dense": w1[n_pairs:],
        "b1": np.ascontiguousarray(np.asarray(inputs["b_top1"]).reshape(-1, P).T),
        "w2": w2,
        "b2": np.ascontiguousarray(np.asarray(inputs["b_top2"]).reshape(-1, P).T),
        "w3": np.ascontiguousarray(w3[:, 0].reshape(-1, P).T),
    }
    nc = bacc.Bacc("TRN2", target_bir_lowering=False, num_devices=1)
    args = [nc.dram_tensor(name, a.shape, mybir.dt.from_np(a.dtype), kind="ExternalInput").ap()
            for name, a in arrays.items()]
    out = nc.dram_tensor("out", (1, ids.shape[0]), F32, kind="ExternalOutput").ap()
    dlrm_tower(nc, *args, out)
    result = run_bass_kernel_spmd(nc, [arrays], core_ids=[0]).results[0]["out"]
    return result.reshape(-1, 1)
```

```python
from contextlib import ExitStack

import concourse.bass as bass
from concourse import mybir

F32 = mybir.dt.float32
F32R = mybir.dt.float32r
I32 = mybir.dt.int32
ALU = mybir.AluOpType
ACT = mybir.ActivationFunctionType

P = 128
QUAD = 32


def table_bases(rows):
    bases, at = [], 0
    for r in rows:
        bases.append(at)
        at += r
    return bases


def dlrm_tower(nc, ids, row_base, tables, ids_small, small_tables, small_rows, spread, dense_t, identity,
               w1_pairs, w1_dense, b1, w2, b2, w3, out):
    FPG, SMALL = P // QUAD, ids_small.shape[0]
    GPF = ids.shape[2]
    F = FPG * GPF + SMALL
    D = tables.shape[1]
    BATCH = ids_small.shape[1]
    H1 = w1_pairs.shape[2]
    H2 = w2.shape[1]
    ND = dense_t.shape[0]
    SPT = P // F
    TPQ, TPG = 4, QUAD // SPT
    GPC, TPC = P // QUAD, P // SPT
    QPG, QPC = TPG // TPQ, TPC // TPQ
    STEPS = GPC * GPF
    PARTS = GPF + 1
    SMALL_AT = 3
    CHUNKS = BATCH // P
    GROUPS = CHUNKS * GPC
    KD = D // P
    JJ = F // FPG
    N1, N2 = H1 // P, H2 // P
    VP, VC = small_rows.shape
    LOADS = 4
    HOT_SLOTS = 4
    BANKS = 3
    LOOKUP_LAG = 2
    EARLY_GROUPS = 2
    EARLY_TURNS = EARLY_GROUPS * GPF + BANKS
    EARLY_PIECE = 8
    GATHER_LAG = 2
    BANK = [s % BANKS for s in range(STEPS - 1)] + [1]
    EARLY_QUADS = 4
    TILES_AT = ([], [0], [1, 2], [3], [4, 5], [6, 7], [])
    QUAD_AT = (4, 6)
    L1_STEP, L2_STEP, L3_STEP = 12, 24, 27
    L1_PACE = 8
    L1_MATMULS = N1 * (JJ + 1)
    EARLY_STEPS = range(GPF * (EARLY_QUADS // QPG + 1) + 2, STEPS)
    LATE_STEPS = range(GPF, GPF + 3)
    H1_STEPS, H2_STEP, Y_STEP = range(L2_STEP - 2, L2_STEP), L2_STEP + N2 - 1, L3_STEP
    FILLERS = 16
    LOOKUP_FILLERS = 12
    WARM_UP = 24
    BLOCKS, ACT_BLOCKS = 16, 6
    MOVES = 2
    assert D == 2 * P and F == QUAD and H1 == 4 * P and L1_STEP + 2 * L1_MATMULS // L1_PACE < L2_STEP
    assert STEPS % BANKS == 1

    with ExitStack() as ctx:
        def sb(name, shape, dt=F32):
            return ctx.enter_context(nc.sbuf_tensor(name, shape, dt))

        def psum(name, shape):
            return ctx.enter_context(nc.psum_tensor(name, shape, F32))

        def sem(name):
            return ctx.enter_context(nc.semaphore(name))

        ids_sb = sb("ids_sb", [P, GROUPS, GPF], I32)
        base_sb = sb("base_sb", [P, GPF])
        idx = sb("idx", [P, (GROUPS + GPC) * GPF], I32)
        idx_now = sb("idx_now", [P, STEPS], I32)
        ids_small_sb = sb("ids_small_sb", [SMALL, BATCH], I32)
        ids_small_r = sb("ids_small_r", [SMALL, BATCH], F32R)
        spread_sb = sb("spread_sb", [SMALL, SMALL, VP])
        spread_r = sb("spread_r", [SMALL, SMALL, VP], F32R)
        small_rows_sb = sb("small_rows_sb", [VP, VC])
        ids_all = sb("ids_all", [VP, SMALL, BATCH])
        small_sb = sb("small_sb", [VP, SMALL, VC, D])
        warm = sb("warm", [P, 2 * P], F32R)
        warm_out = sb("warm_out", [P, 1])
        small_hi = sb("small_hi", [VP, HOT_SLOTS, D], F32R)
        small_lo = sb("small_lo", [VP, HOT_SLOTS, D], F32R)
        one_hot = sb("one_hot", [VP, HOT_SLOTS, BATCH], F32R)
        looked_up = sb("looked_up", [P, KD, SMALL, BATCH])
        ident = sb("ident", [P, P])
        rows = sb("rows", [P, STEPS, D])
        hi_lo = sb("hi_lo", [P, 2, KD, 2, QUAD * F], F32R)
        hi_hi = sb("hi_hi", [P, 2, TPQ, P])
        sums = sb("sums", [P, TPC, P])
        pairs = sb("pairs", [P, JJ, P])
        w1_sb = sb("w1_sb", [P, JJ, H1])
        w1d_sb = sb("w1d_sb", [ND, H1])
        dense_sb = sb("dense_sb", [ND, BATCH])
        b1_sb = sb("b1_sb", [P, N1])
        w2_sb = sb("w2_sb", [P, N1, H2])
        b2_sb = sb("b2_sb", [P, N2])
        w3_sb = sb("w3_sb", [P, N2])
        h1 = sb("h1", [P, N1, P])
        h2 = sb("h2", [P, N2, P])
        y = sb("y", [1, BATCH])

        turned = psum("turned", [P, BANKS, 2 * KD, P])
        gram = psum("gram", [P, 2, TPQ, 2, P])
        p1 = psum("p1", [P, N1, P])

        ids_in = sem("ids_in")
        base_in = sem("base_in")
        warm_ready = sem("warm_ready")
        small_ids_in = sem("small_ids_in")
        small_in = [sem(f"small_in{n}") for n in range(LOADS)]
        ident_in = sem("ident_in")
        weights_in = sem("weights_in")
        idx_made = sem("idx_made")
        idx_ready = sem("idx_ready")
        small_ids_ready = sem("small_ids_ready")
        ids_spread = sem("ids_spread")
        ids_all_ready = sem("ids_all_ready")
        small_rounded = sem("small_rounded")
        small_split = sem("small_split")
        small_used = sem("small_used")
        looked_act = sem("looked_act")
        looked_dve = sem("looked_dve")
        row_in = [sem(f"row_in{s}") for s in range(STEPS)]
        turned_ready = sem("turned_ready")
        parts_rounded = sem("parts_rounded")
        parts_split = sem("parts_split")
        quads_multiplied = sem("quads_multiplied")
        quads_copied = sem("quads_copied")
        quads_summed = sem("quads_summed")
        moved_act = sem("moved_act")
        moved_dve = sem("moved_dve")
        p1_done = sem("p1_done")
        h1_ready = sem("h1_ready")
        p2_done = sem("p2_done")
        h2_ready = sem("h2_ready")
        p3_done = sem("p3_done")
        y_ready = sem("y_ready")
        out_done = sem("out_done")
        SUM_START, MUL_START = 2, 2 * QPG
        WEIGHT_DMAS = 7
        block = ctx.enter_context(nc.Block())

        def move_pairs(copy, late, n, of, blocks):
            t0, t1 = ((0, EARLY_QUADS * TPQ), (EARLY_QUADS * TPQ, TPC))[late]
            blocks = blocks[n * len(blocks) // of:(n + 1) * len(blocks) // of]
            for m in blocks:
                g, q = m // (P // QUAD), m % (P // QUAD)
                src = sums[QUAD * g:QUAD * (g + 1), t0:t1, QUAD * g + JJ * q:QUAD * g + JJ * (q + 1)]
                dst = pairs[QUAD * q:QUAD * (q + 1), :, SPT * t0 + g:SPT * t1:SPT].rearrange("p j t -> p t j")
                last = copy(dst, src)
            return last

        def gathered_part(g, j, which):
            part = hi_lo[:, g % 2, :, which, :].rearrange("p k (b f) -> p k b f", f=F)
            return part[:, :, :, j * FPG:(j + 1) * FPG]

        def small_part(g, which):
            return hi_lo[:, g % 2, :, which, :].rearrange("p k (b f) -> p k b f", f=F)[:, :, :, F - SMALL:]

        def turned_rows(s):
            return turned[:, BANK[s], 0:KD, :].rearrange("p k (f b) -> p k b f", f=FPG)

        def looked_rows(c, g):
            return looked_up[:, :, :, bass.ds(c * P + g * QUAD, QUAD)].rearrange("p k f b -> p k b f")

        def parts_before(s):
            return s // GPF * PARTS + s % GPF + (1 if s % GPF >= SMALL_AT else 0)

        def lookup_bank(k, kd):
            return gram[:, k % 2, kd * 2:kd * 2 + 2, :, :].rearrange("p t a b -> p (t a b)")

        def spread_bank(k):
            bank = (p1[0:VP, :, :], *(turned[0:VP, n, :, :] for n in range(BANKS)))[k]
            return bank.rearrange("p a b -> p (a b)")

        def last_p1(n):
            return gram[:, n // 2, n % 2 * (TPQ // 2), 0, :]

        def last_p2(n):
            return (p1[:, 0, :], turned[:, 2, 0, :])[n]

        last_p3 = turned[0:1, 0, 0, :]

        @block.sync
        def _(sp):
            sp.dma_start(ids_sb[:, :, :], ids).then_inc(ids_in, 16)
            sp.dma_start(ids_small_sb[:, :], ids_small).then_inc(small_ids_in, 16)
            for k in range(SMALL):
                for n in range(LOADS):
                    if k:
                        sp.wait_ge(small_in[n], 16 * k)
                    pieces = slice(n * (VC // LOADS), (n + 1) * (VC // LOADS))
                    sp.dma_start(small_sb[:, k, pieces, :], small_tables[k, :, pieces, :]).then_inc(small_in[n], 16)
            sp.dma_start(w1_sb[:, :, :], w1_pairs).then_inc(weights_in, 16)
            sp.dma_start(w2_sb[:, :, :], w2.rearrange("(k p) n -> p k n", p=P)).then_inc(weights_in, 16)
            sp.dma_start(dense_sb[:, :], dense_t).then_inc(weights_in, 16)
            sp.dma_start(w1d_sb[:, :], w1_dense).then_inc(weights_in, 16)
            sp.dma_start(b1_sb[:, :], b1).then_inc(weights_in, 16)
            sp.dma_start(b2_sb[:, :], b2).then_inc(weights_in, 16)
            sp.dma_start(w3_sb[:, :], w3).then_inc(weights_in, 16)
            sp.wait_ge(y_ready, 1 + CHUNKS)
            sp.dma_start(out, y[:, :]).then_inc(out_done, 16)
            sp.wait_ge(out_done, 16)

        @block.gpsimd
        def _(pool):
            with pool.Fori(0, CHUNKS) as c:
                for s in range(STEPS):
                    if s % GPF == 0:
                        pool.wait_ge(idx_ready, c * GPC + s // GPF + 1)
                        nc.gpsimd.nop(nofuse=True)
                    pool.indirect_dma_start(rows[:, s, :], None, tables,
                                            bass.IndirectOffsetOnAxis(idx_now[:, s:s + 1], 0)).then_inc(row_in[s], 16)

        @block.tensor
        def _(pe):
            def turn(c, s, first):
                g, j = s // GPF, s % GPF
                if first and s < EARLY_TURNS:
                    if s >= BANKS:
                        pe.wait_ge(parts_split, s - BANKS + 1)
                elif s >= BANKS:
                    last_user = max(n for n in range(s) if BANK[n] == BANK[s])
                    pe.wait_ge(parts_split, c * (PARTS * GPC) + (parts_before(last_user) + 1))
                else:
                    last_user = max(n for n in range(STEPS) if BANK[n] == BANK[s])
                    pe.wait_ge(parts_split, (c - 1) * (PARTS * GPC) + (parts_before(last_user) + 1))
                pe.wait_ge(row_in[s], c * 16 + 16)
                for kd in range(KD):
                    last = nc.tensor.transpose(turned[:, BANK[s], kd, :], rows[:, s, kd * P:(kd + 1) * P], ident[:, :])
                last.then_inc(turned_ready, 1)

            def multiply(c, g, t, first):
                if t == 0:
                    parts = EARLY_GROUPS * GPF + g + 1 if first and g < EARLY_GROUPS else (g + 1) * PARTS
                    pe.wait_ge(parts_split, c * (PARTS * GPC) + parts)
                if t % TPQ == 0:
                    pe.wait_ge(quads_summed, c * QPC + QPG * g + t // TPQ + 1)
                cols = slice(t * P, (t + 1) * P)
                for kd in range(KD):
                    last = nc.tensor.matmul(gram[:, t // TPQ, t % TPQ, :, :], hi_lo[:, g % 2, kd, 0, cols],
                                            hi_lo[:, g % 2, kd, :, cols], start=(kd == 0), stop=(kd == KD - 1))
                if t % TPQ == TPQ - 1:
                    last.then_inc(quads_multiplied, 1)

            def look_up(k):
                for v in range(VC):
                    piece = k * VC + v
                    pe.wait_ge(small_split, piece + 1)
                    for part, operand in enumerate((small_hi, small_lo)):
                        for kd in range(KD):
                            if v == 0 and part == 0 and k >= 2:
                                pe.wait_ge((looked_act, looked_dve)[kd], k - 1)
                            last = nc.tensor.matmul(lookup_bank(k, kd),
                                                    operand[:, piece % HOT_SLOTS, kd * P:(kd + 1) * P],
                                                    one_hot[:, piece % HOT_SLOTS, :],
                                                    start=(v == 0 and part == 0), stop=(v == VC - 1 and part == 1))
                    last.then_inc(small_used, 1)
                    if piece == EARLY_PIECE:
                        pe.wait_ge(ident_in, 16)
                        pe.wait_ge(ids_all_ready, SMALL)
                    if 0 <= piece - EARLY_PIECE < EARLY_GROUPS * GPF:
                        turn(0, piece - EARLY_PIECE, True)

            def first_layer(c, m0, m1):
                for m in range(m0, min(m1, L1_MATMULS)):
                    if m == 0:
                        pe.wait_ge(weights_in, 16 * WEIGHT_DMAS)
                        pe.wait_ge(y_ready, c + 1)
                        pe.wait_ge(moved_act, c * MOVES + MOVES)
                        pe.wait_ge(moved_dve, c * MOVES + MOVES)
                    n, k = m // (JJ + 1), m % (JJ + 1)
                    cols = slice(n * P, (n + 1) * P)
                    if k == 0:
                        nc.tensor.matmul(p1[:, n, :], w1d_sb[:, cols], dense_sb[:, bass.ds(c * P, P)],
                                         start=True, stop=False)
                        continue
                    last = nc.tensor.matmul(p1[:, n, :], w1_sb[:, k - 1, cols], pairs[:, k - 1, :],
                                            start=False, stop=(k == JJ))
                    if m == L1_MATMULS - 1:
                        last.then_inc(p1_done, 1)

            def second_layer(c, n):
                if n == 0:
                    pe.wait_ge(h1_ready, c + 1)
                for k in range(N1):
                    last = nc.tensor.matmul(p1[:, n, :], w2_sb[:, k, n * P:(n + 1) * P], h1[:, k, :],
                                            start=(k == 0), stop=(k == N1 - 1))
                if n == N2 - 1:
                    last.then_inc(p2_done, 1)

            def third_layer(c):
                pe.wait_ge(h2_ready, c + 1)
                for k in range(N2):
                    last = nc.tensor.matmul(p1[0:1, 2, :], w3_sb[:, k:k + 1], h2[:, k, :],
                                            start=(k == 0), stop=(k == N2 - 1))
                last.then_inc(p3_done, 1)

            def chunk(c, first):
                for s in range(STEPS):
                    g, j = s // GPF, s % GPF
                    if not first or s >= EARLY_TURNS:
                        turn(c, s, first)
                    for t in TILES_AT[j]:
                        if g:
                            multiply(c, g - 1, t, first)
                        elif not first:
                            multiply(c - 1, GPC - 1, t, False)
                    if not first and s >= L1_STEP:
                        first_layer(c - 1, (s - L1_STEP) * L1_PACE // 2, (s - L1_STEP + 1) * L1_PACE // 2)
                    if not first and L2_STEP <= s < L2_STEP + N2:
                        second_layer(c - 1, s - L2_STEP)
                    if not first and s == L3_STEP:
                        third_layer(c - 1)

            nc.tensor.sem_inc(quads_multiplied, MUL_START)
            nc.tensor.sem_inc(p1_done, 1)
            pe.wait_ge(warm_ready, 1)
            for _ in range(WARM_UP):
                nc.tensor.matmul(turned[:, 0, 0:2, :], warm[:, 0:P], warm[:, :], start=True, stop=True)
            pe.wait_ge(small_ids_ready, 2)
            for k in range(SMALL):
                nc.tensor.matmul(spread_bank(k), spread_r[:, k, :], ids_small_r[:, :],
                                 start=True, stop=True).then_inc(ids_spread, 1)
            for k in range(SMALL):
                look_up(k)
            for s in range(EARLY_GROUPS * GPF, EARLY_TURNS):
                turn(0, s, True)
            for _ in range(LOOKUP_FILLERS):
                nc.tensor.matmul(p1[:, 0:2, :], warm[:, 0:P], warm[:, :], start=True, stop=True)
            pe.wait_ge(looked_act, SMALL)
            pe.wait_ge(looked_dve, SMALL)
            chunk(0, True)
            with pe.Fori(1, CHUNKS) as c:
                chunk(c, False)
            c = CHUNKS - 1
            for t in range(TPG):
                multiply(c, GPC - 1, t, False)
            for _ in range(FILLERS):
                nc.tensor.matmul(turned[:, 0, 0:2, :].rearrange("p a b -> p (a b)"), hi_lo[:, 0, 0, 0, 0:P],
                                 hi_lo[:, 0, 0, 0, 0:2 * P], start=True, stop=True)
            pe.wait_ge(moved_act, c * MOVES + MOVES)
            pe.wait_ge(moved_dve, c * MOVES + MOVES)
            for n in range(N1):
                cols = slice(n * P, (n + 1) * P)
                nc.tensor.matmul(last_p1(n), w1d_sb[:, cols], dense_sb[:, c * P:(c + 1) * P], start=True, stop=False)
                for k in range(JJ):
                    last = nc.tensor.matmul(last_p1(n), w1_sb[:, k, cols], pairs[:, k, :],
                                            start=False, stop=(k == JJ - 1))
                last.then_inc(p1_done, 1)
            pe.wait_ge(y_ready, c + 1)
            for k in range(N1):
                pe.wait_ge(h1_ready, c + k + 1)
                for n in range(N2):
                    last = nc.tensor.matmul(last_p2(n), w2_sb[:, k, n * P:(n + 1) * P], h1[:, k, :],
                                            start=(k == 0), stop=(k == N1 - 1))
                    if k == N1 - 1:
                        last.then_inc(p2_done, 1)
            for k in range(N2):
                pe.wait_ge(h2_ready, c + k + 1)
                last = nc.tensor.matmul(last_p3, w3_sb[:, k:k + 1], h2[:, k, :], start=(k == 0), stop=(k == N2 - 1))
            last.then_inc(p3_done, 1)


        @block.scalar
        def _(act):
            def copy(dst, src):
                return nc.scalar.activation(dst, src, ACT.Copy)

            def round_gather(c, s):
                g, j = s // GPF, s % GPF
                if j == 0:
                    act.wait_ge(quads_multiplied, c * QPC + QPG * (g + 1))
                act.wait_ge(turned_ready, c * STEPS + s + 1)
                copy(gathered_part(g, j, 0), turned_rows(s)).then_inc(parts_rounded, 1)

            def round_small(c, g):
                copy(small_part(g, 0), looked_rows(c, g)).then_inc(parts_rounded, 1)

            def copy_quad(c, q):
                act.wait_ge(quads_summed, c * QPC + q + 1)
                act.wait_ge(quads_multiplied, c * QPC + (MUL_START + q + 1))
                copy(hi_hi[:, q % 2, :, :], gram[:, q % 2, :, 0, :]).then_inc(quads_copied, 1)

            def move(c, late, n, of):
                if n == 0 and not late:
                    act.wait_ge(p1_done, c + 1)
                if n == 0:
                    act.wait_ge(quads_summed, c * QPC + (SUM_START + (EARLY_QUADS, QPC)[late]))
                last = move_pairs(copy, late, n, of, range(0, ACT_BLOCKS))
                if n == of - 1:
                    last.then_inc(moved_act, 1)

            def finish_h1(c, n0, n1):
                if n0 == 0:
                    act.wait_ge(weights_in, 16 * WEIGHT_DMAS)
                    act.wait_ge(p1_done, c + 2)
                for n in range(n0, n1):
                    last = nc.scalar.activation(h1[:, n, :], p1[:, n, :], ACT.Relu, bias=b1_sb[:, n:n + 1])
                if n1 == N1:
                    last.then_inc(h1_ready, 1)

            def copy_ids(k):
                act.wait_ge(ids_spread, k + 1)
                copy(ids_all[:, k, :], spread_bank(k)).then_inc(ids_all_ready, 1)

            def round_small_table(k):
                for v in range(VC):
                    piece = k * VC + v
                    if k == 0 and v % 2 == 0:
                        copy_ids(v // 2)
                    if v % (VC // LOADS) == 0:
                        act.wait_ge(small_in[v * LOADS // VC], k * 16 + 16)
                    if piece >= HOT_SLOTS:
                        act.wait_ge(small_used, piece - HOT_SLOTS + 1)
                    copy(small_hi[:, piece % HOT_SLOTS, :], small_sb[:, k, v, :]).then_inc(small_rounded, 1)
                    if v == LOOKUP_LAG and k:
                        copy_looked(k - 1)
                    if 0 <= piece - GATHER_LAG - EARLY_PIECE < EARLY_GROUPS * GPF:
                        round_gather(0, piece - GATHER_LAG - EARLY_PIECE)

            def copy_looked(k):
                act.wait_ge(small_used, k * VC + VC)
                copy(looked_up[:, 0, k, :], lookup_bank(k, 0)).then_inc(looked_act, 1)

            def chunk(c, first):
                for s in range(STEPS):
                    g, j = s // GPF, s % GPF
                    if j == SMALL_AT and (not first or g >= EARLY_GROUPS):
                        round_small(c, g)
                    if not first or g >= EARLY_GROUPS:
                        round_gather(c, s)
                    if j in QUAD_AT and not (first and g == 0):
                        q = QUAD_AT.index(j)
                        if g:
                            copy_quad(c, QPG * (g - 1) + q)
                        else:
                            copy_quad(c - 1, QPG * (GPC - 1) + q)
                    if s in LATE_STEPS and not first:
                        move(c - 1, True, LATE_STEPS.index(s), len(LATE_STEPS))
                    if s in H1_STEPS and not first:
                        n = H1_STEPS.index(s) * N1 // len(H1_STEPS)
                        finish_h1(c - 1, n, n + N1 // len(H1_STEPS))
                    if s in EARLY_STEPS:
                        move(c, False, EARLY_STEPS.index(s), len(EARLY_STEPS))

            act.dma_start(base_sb[:, :], row_base).then_inc(base_in, 16)
            act.dma_start(spread_sb[:, :, :], spread).then_inc(small_ids_in, 16)
            act.dma_start(small_rows_sb[:, :], small_rows).then_inc(small_ids_in, 16)
            act.dma_start(ident[:, :], identity).then_inc(ident_in, 16)
            act.wait_ge(warm_ready, 1)
            copy(warm_out[:, :], warm[:, 0:1].bitcast(F32))
            for k in range(SMALL):
                round_small_table(k)
            copy_looked(SMALL - 1)
            act.wait_ge(looked_act, SMALL)
            act.wait_ge(looked_dve, SMALL)
            for g in range(EARLY_GROUPS):
                round_small(0, g)
            chunk(0, True)
            with act.Fori(1, CHUNKS) as c:
                chunk(c, False)
            copy_quad(CHUNKS - 1, QPC - 2)
            copy_quad(CHUNKS - 1, QPC - 1)
            move(CHUNKS - 1, True, 0, 1)

        @block.vector
        def _(dve):
            def split_gather(c, s, first):
                g, j = s // GPF, s % GPF
                before = s if first and g < EARLY_GROUPS else parts_before(s)
                dve.wait_ge(parts_rounded, c * (PARTS * GPC) + (before + 1))
                nc.vector.tensor_tensor(gathered_part(g, j, 1), turned_rows(s), gathered_part(g, j, 0).bitcast(F32),
                                        ALU.subtract).then_inc(parts_split, 1)

            def split_small(c, g, first):
                before = EARLY_GROUPS * GPF + g if first and g < EARLY_GROUPS else PARTS * g + SMALL_AT
                dve.wait_ge(parts_rounded, c * (PARTS * GPC) + (before + 1))
                nc.vector.tensor_tensor(small_part(g, 1), looked_rows(c, g), small_part(g, 0).bitcast(F32),
                                        ALU.subtract).then_inc(parts_split, 1)

            def renew_idx(c, g):
                nc.vector.tensor_copy(idx_now[:, g * GPF:(g + 1) * GPF],
                                      idx[:, bass.ds(c * STEPS + (STEPS + g * GPF), GPF)]).then_inc(idx_ready, 1)

            def sum_quad(c, q, first):
                if not first and q == 0:
                    dve.wait_ge(moved_act, c * MOVES - 1)
                if not first and q == EARLY_QUADS:
                    dve.wait_ge(moved_act, c * MOVES)
                dve.wait_ge(quads_copied, c * QPC + q + 1)
                nc.vector.scalar_tensor_tensor(out=sums[:, q * TPQ:(q + 1) * TPQ, :], in0=hi_hi[:, q % 2, :, :],
                                               scalar=0.5, in1=gram[:, q % 2, :, 1, :], op0=ALU.mult,
                                               op1=ALU.add).then_inc(quads_summed, 1)

            def move(c, late, n, of):
                if n == 0 and not late:
                    dve.wait_ge(p1_done, c + 1)
                if n == 0:
                    dve.wait_ge(quads_summed, c * QPC + (SUM_START + (EARLY_QUADS, QPC)[late]))
                last = move_pairs(nc.vector.tensor_copy, late, n, of, range(ACT_BLOCKS, BLOCKS))
                if n == of - 1:
                    last.then_inc(moved_dve, 1)

            def finish_h2(c):
                dve.wait_ge(weights_in, 16 * WEIGHT_DMAS)
                dve.wait_ge(p2_done, c + 1)
                for n in range(N2):
                    last = nc.vector.tensor_scalar(h2[:, n, :], p1[:, n, :], b2_sb[:, n:n + 1], 0.0, ALU.add, ALU.max)
                last.then_inc(h2_ready, 1)

            def finish_y(c):
                dve.wait_ge(p3_done, c + 1)
                nc.vector.tensor_copy(y[:, bass.ds(c * P, P)], p1[0:1, 2, :]).then_inc(y_ready, 1)

            def split_small_table(k):
                dve.wait_ge(ids_all_ready, k + 1)
                for v in range(VC):
                    piece = k * VC + v
                    if piece >= HOT_SLOTS:
                        dve.wait_ge(small_used, piece - HOT_SLOTS + 1)
                    nc.vector.tensor_scalar(one_hot[:, piece % HOT_SLOTS, :], ids_all[:, k, :],
                                            small_rows_sb[:, v:v + 1], None, ALU.is_equal)
                    dve.wait_ge(small_rounded, piece + 1)
                    nc.vector.tensor_tensor(small_lo[:, piece % HOT_SLOTS, :], small_sb[:, k, v, :],
                                            small_hi[:, piece % HOT_SLOTS, :].bitcast(F32), ALU.subtract
                                            ).then_inc(small_split, 1)
                    if v == LOOKUP_LAG and k:
                        copy_looked(k - 1)
                    s = piece - GATHER_LAG - EARLY_PIECE
                    if 0 <= s < EARLY_GROUPS * GPF:
                        split_gather(0, s, True)
                        if s % GPF == GPF - 1:
                            renew_idx(0, s // GPF)

            def copy_looked(k):
                dve.wait_ge(small_used, k * VC + VC)
                nc.vector.tensor_copy(looked_up[:, 1, k, :], lookup_bank(k, 1)).then_inc(looked_dve, 1)

            def chunk(c, first):
                for s in range(STEPS):
                    g, j = s // GPF, s % GPF
                    if j == SMALL_AT and (not first or g >= EARLY_GROUPS):
                        split_small(c, g, first)
                    if not first or g >= EARLY_GROUPS:
                        split_gather(c, s, first)
                        if j == GPF - 1:
                            renew_idx(c, g)
                    if j in QUAD_AT and not (first and g == 0):
                        q = QUAD_AT.index(j)
                        if g:
                            sum_quad(c, QPG * (g - 1) + q, first)
                        else:
                            sum_quad(c - 1, QPG * (GPC - 1) + q, False)
                    if s in LATE_STEPS and not first:
                        move(c - 1, True, LATE_STEPS.index(s), len(LATE_STEPS))
                    if s == H2_STEP and not first:
                        finish_h2(c - 1)
                    if s in EARLY_STEPS:
                        move(c, False, EARLY_STEPS.index(s), len(EARLY_STEPS))
                    if s == Y_STEP and not first:
                        finish_y(c - 1)

            nc.vector.memset(warm[:, :].bitcast(F32), 0.0).then_inc(warm_ready, 1)
            nc.vector.sem_inc(quads_summed, SUM_START)
            nc.vector.sem_inc(y_ready, 1)
            nc.vector.memset(idx[:, GROUPS * GPF:], 0)
            dve.wait_ge(ids_in, 16)
            dve.wait_ge(base_in, 16)
            nc.vector.tensor_tensor(idx_now[:, 0:GPF], ids_sb[:, 0, :], base_sb[:, :], ALU.add).then_inc(idx_ready, 1)
            nc.vector.tensor_tensor(idx[:, 0:GROUPS * GPF].rearrange("p (g j) -> p g j", j=GPF), ids_sb[:, :, :],
                                    base_sb[:, None, :].broadcast_to([P, GROUPS, GPF]), ALU.add).then_inc(idx_made, 1)
            dve.wait_ge(small_ids_in, 48)
            nc.vector.tensor_copy(ids_small_r[:, :], ids_small_sb[:, :]).then_inc(small_ids_ready, 1)
            nc.vector.tensor_copy(spread_r[:, :, :], spread_sb[:, :, :]).then_inc(small_ids_ready, 1)
            dve.wait_ge(idx_made, 1)
            nc.vector.tensor_copy(idx_now[:, GPF:], idx[:, GPF:STEPS]).then_inc(idx_ready, GPC - 1)
            for k in range(SMALL):
                split_small_table(k)
            copy_looked(SMALL - 1)
            dve.wait_ge(looked_act, SMALL)
            dve.wait_ge(looked_dve, SMALL)
            for g in range(EARLY_GROUPS):
                split_small(0, g, True)
            chunk(0, True)
            with dve.Fori(1, CHUNKS) as c:
                chunk(c, False)
            sum_quad(CHUNKS - 1, QPC - 2, False)
            sum_quad(CHUNKS - 1, QPC - 1, False)
            move(CHUNKS - 1, True, 0, 1)
            c = CHUNKS - 1
            for n in range(N1):
                dve.wait_ge(p1_done, c + n + 2)
                nc.vector.tensor_scalar(h1[:, n, :], last_p1(n), b1_sb[:, n:n + 1], 0.0, ALU.add,
                                        ALU.max).then_inc(h1_ready, 1)
            for n in range(N2):
                dve.wait_ge(p2_done, c + n + 1)
                nc.vector.tensor_scalar(h2[:, n, :], last_p2(n), b2_sb[:, n:n + 1], 0.0, ALU.add,
                                        ALU.max).then_inc(h2_ready, 1)
            dve.wait_ge(p3_done, c + 1)
            nc.vector.tensor_copy(y[:, c * P:], last_p3).then_inc(y_ready, 1)


def kernel(**inputs):
    import numpy as np
    import concourse.bacc as bacc
    from concourse.bass_utils import run_bass_kernel_spmd

    n_small, pieces = 4, 8
    ids = np.asarray(inputs["ids"])
    batch, fields = ids.shape
    tables = [np.asarray(inputs[f"tbl_{f}"]) for f in range(fields)]
    w1, w2, w3 = (np.asarray(inputs[f"W_top{n}"]) for n in (1, 2, 3))
    n_pairs = fields * (fields - 1) // 2
    by_size = sorted(range(fields), key=lambda f: len(tables[f]))
    small = sorted(by_size[:n_small])
    gathered = [f for f in range(fields) if f not in small]
    at = np.array(gathered + small)
    v = len(tables[small[0]])
    assert all(len(tables[f]) == v for f in small) and v % pieces == 0 and v // pieces <= P
    per_gather = P // QUAD
    ids_gathered = ids[:, gathered].reshape(batch // QUAD, QUAD, -1, per_gather).transpose(3, 1, 0, 2)
    base = np.array(table_bases([len(tables[f]) for f in gathered]), np.float32)
    i, j = np.meshgrid(at, at, indexing="ij")
    a, b = np.minimum(i, j), np.maximum(i, j)
    row = np.where(i == j, n_pairs, a * fields - a * (a + 1) // 2 + b - a - 1)
    padded = np.concatenate([w1[:n_pairs], np.zeros((1, w1.shape[1]), w1.dtype)])
    order = row.reshape(fields, P // QUAD, -1).transpose(1, 0, 2).reshape(P, -1)

    arrays = {
        "ids": np.ascontiguousarray(ids_gathered.reshape(P, batch // QUAD, -1)),
        "row_base": np.repeat(base.reshape(-1, per_gather).T, QUAD, axis=0),
        "tables": np.concatenate([tables[f] for f in gathered]),
        "ids_small": np.ascontiguousarray(ids[:, small].T),
        "small_tables": np.stack([tables[f] for f in small]).reshape(n_small, v // pieces, pieces, -1),
        "small_rows": np.arange(v, dtype=np.float32).reshape(-1, pieces),
        "spread": np.repeat(np.eye(n_small, dtype=np.float32)[:, :, None], v // pieces, axis=2),
        "dense_t": np.ascontiguousarray(np.asarray(inputs["dense_ctx"]).T),
        "identity": np.eye(P, dtype=np.float32),
        "w1_pairs": padded[order],
        "w1_dense": w1[n_pairs:],
        "b1": np.ascontiguousarray(np.asarray(inputs["b_top1"]).reshape(-1, P).T),
        "w2": w2,
        "b2": np.ascontiguousarray(np.asarray(inputs["b_top2"]).reshape(-1, P).T),
        "w3": np.ascontiguousarray(w3[:, 0].reshape(-1, P).T),
    }
    nc = bacc.Bacc("TRN2", target_bir_lowering=False, num_devices=1)
    args = [nc.dram_tensor(name, a.shape, mybir.dt.from_np(a.dtype), kind="ExternalInput").ap()
            for name, a in arrays.items()]
    out = nc.dram_tensor("out", (1, batch), F32, kind="ExternalOutput").ap()
    dlrm_tower(nc, *args, out)
    result = run_bass_kernel_spmd(nc, [arrays], core_ids=[0]).results[0]["out"]
    return result.reshape(-1, 1)
```
